# Optimizing a Trainium2 kernel written in Bass

```python
import numpy as np
import jax
import jax.numpy as jnp

def _softmax(x, axis=-1):
    return jax.nn.softmax(x, axis=axis)

def _gelu(x):
    return jax.nn.gelu(x, approximate=True)

def _silu(x):
    return jax.nn.silu(x)

def _sigmoid(x):
    return jax.nn.sigmoid(x)

def _layernorm(x, axis=-1, eps=1e-05):
    m = jnp.mean(x, axis=axis, keepdims=True)
    v = jnp.var(x, axis=axis, keepdims=True)
    return (x - m) / jnp.sqrt(v + eps)

def _scatter_add(tgt, idx, src, axis=0):
    return tgt.at[idx].add(src)

def _segment_sum(src, seg, n):
    return jax.ops.segment_sum(src, seg, n)
kernel_name = 'mk_lm_tower_d1_tok_ids512_r4_6a2ec4'

def setup_inputs(seed: int=0):
    np.random.seed(seed)
    _w = jnp.asarray

    def _rec_inputs():
        import jax
        import jax.numpy as jnp
        _rk = jax.random.key(seed)
        x = jax.random.randint(jax.random.fold_in(_rk, 1), (8, 256), 0, 50257, jnp.int32)
        return x
    x = _rec_inputs()

    def _L0_tok_setup():
        import jax, jax.numpy as jnp
        import numpy as np
        D_MODEL = 128
        VOCAB = 50257
        BATCH = 8
        SEQ = 512

        def _positional_encoding(seq_len, d_model, dtype):
            pos = jnp.arange(1, seq_len + 1, dtype=jnp.float32)[:, None]
            i = jnp.arange(d_model)
            exponent = jnp.where(i % 2 == 0, i, i + 1).astype(jnp.float32) / d_model
            angle = pos / 10000.0 ** exponent
            pe = jnp.where(i % 2 == 0, jnp.cos(angle), jnp.sin(angle))
            return pe.astype(dtype)
        key = jax.random.key(seed)
        k1, k2, k3 = jax.random.split(key, 3)
        x = jax.random.randint(k1, (BATCH, SEQ), 0, VOCAB)
        W = jax.random.normal(k2, (D_MODEL, VOCAB), dtype=jnp.float32) * 0.02
        b = jax.random.normal(k3, (D_MODEL,), dtype=jnp.float32) * 0.02
        return {'x': x, 'W': W, 'b': b}
    _L0_tok_all = _L0_tok_setup()
    _L0_tok_in = {k: v for k, v in _L0_tok_all.items() if k in ('W', 'b')}
    del _L0_tok_all

    def _L0_attn_setup():
        import jax, jax.numpy as jnp
        import numpy as np
        BSZ, L, H, P = (8, 1024, 128, 64)
        DT_MIN, DT_MAX = (0.001, 0.1)

        def _binop(q_i, q_j):
            A_i, b_i = q_i
            A_j, b_j = q_j
            return (A_j * A_i, A_j * b_i + b_j)
        key = jax.random.key(seed)
        k_u, k_B, k_C, k_D, k_dt = jax.random.split(key, 5)
        u = jax.random.normal(k_u, (BSZ, L, H), dtype=jnp.float32)
        Lambda_re = -0.5 * jnp.ones((P,), dtype=jnp.float32)
        Lambda_im = jnp.pi * jnp.arange(P, dtype=jnp.float32)
        B = jax.random.normal(k_B, (P, H, 2), dtype=jnp.float32) / jnp.sqrt(2.0 * H)
        C = jax.random.normal(k_C, (H, P, 2), dtype=jnp.float32) / jnp.sqrt(2.0 * P)
        D = jax.random.normal(k_D, (H,), dtype=jnp.float32)
        log_step = jax.random.uniform(k_dt, (P, 1), dtype=jnp.float32, minval=jnp.log(DT_MIN), maxval=jnp.log(DT_MAX))
        return {'u': u, 'Lambda_re': Lambda_re, 'Lambda_im': Lambda_im, 'B': B, 'C': C, 'D': D, 'log_step': log_step}
    _L0_attn_all = _L0_attn_setup()
    _L0_attn_in = {k: v for k, v in _L0_attn_all.items() if k in ('Lambda_re', 'Lambda_im', 'B', 'C', 'D', 'log_step')}
    del _L0_attn_all

    def _L0_ffn_setup():
        import jax, jax.numpy as jnp
        import numpy as np
        TOP_K = 2
        key = jax.random.key(seed)
        ks = jax.random.split(key, 4)
        b, t, d, e, h = (2, 512, 128, 8, 256)
        scale = 0.02
        return {'x': jax.random.normal(ks[0], (b, t, d), dtype=jnp.float32), 'router_w': jax.random.normal(ks[1], (e, d), dtype=jnp.float32) * scale, 'router_b': jnp.zeros((e,), dtype=jnp.float32), 'fc1_w': jax.random.normal(ks[2], (e, 2 * h, d), dtype=jnp.float32) * scale, 'fc1_b': jnp.zeros((e, 2 * h), dtype=jnp.float32), 'fc2_w': jax.random.normal(ks[3], (e, d, h), dtype=jnp.float32) * scale, 'fc2_b': jnp.zeros((e, d), dtype=jnp.float32)}
    _L0_ffn_all = _L0_ffn_setup()
    _L0_ffn_in = {k: v for k, v in _L0_ffn_all.items() if k in ('router_w', 'router_b', 'fc1_w', 'fc1_b', 'fc2_w', 'fc2_b')}
    del _L0_ffn_all
    return {'x': x, 'L0_tok_W': _L0_tok_in['W'], 'L0_tok_b': _L0_tok_in['b'], 'L0_attn_Lambda_re': _L0_attn_in['Lambda_re'], 'L0_attn_Lambda_im': _L0_attn_in['Lambda_im'], 'L0_attn_B': _L0_attn_in['B'], 'L0_attn_C': _L0_attn_in['C'], 'L0_attn_D': _L0_attn_in['D'], 'L0_attn_log_step': _L0_attn_in['log_step'], 'L0_ffn_router_w': _L0_ffn_in['router_w'], 'L0_ffn_router_b': _L0_ffn_in['router_b'], 'L0_ffn_fc1_w': _L0_ffn_in['fc1_w'], 'L0_ffn_fc1_b': _L0_ffn_in['fc1_b'], 'L0_ffn_fc2_w': _L0_ffn_in['fc2_w'], 'L0_ffn_fc2_b': _L0_ffn_in['fc2_b']}

def reference(x, L0_tok_W, L0_tok_b, L0_attn_Lambda_re, L0_attn_Lambda_im, L0_attn_B, L0_attn_C, L0_attn_D, L0_attn_log_step, L0_ffn_router_w, L0_ffn_router_b, L0_ffn_fc1_w, L0_ffn_fc1_b, L0_ffn_fc2_w, L0_ffn_fc2_b):
    import jax
    import jax.numpy as jnp

    def _L0_tok_ref(x, W, b):
        import jax, jax.numpy as jnp
        import numpy as np
        D_MODEL = 128
        VOCAB = 50257
        BATCH = 8
        SEQ = 512

        def _positional_encoding(seq_len, d_model, dtype):
            pos = jnp.arange(1, seq_len + 1, dtype=jnp.float32)[:, None]
            i = jnp.arange(d_model)
            exponent = jnp.where(i % 2 == 0, i, i + 1).astype(jnp.float32) / d_model
            angle = pos / 10000.0 ** exponent
            pe = jnp.where(i % 2 == 0, jnp.cos(angle), jnp.sin(angle))
            return pe.astype(dtype)
        emb = jnp.take(W.T, x, axis=0) + b
        pe = _positional_encoding(x.shape[1], W.shape[0], emb.dtype)
        return emb + pe[None, :, :]

    def _L0_attn_ref(u, Lambda_re, Lambda_im, B, C, D, log_step):
        import jax, jax.numpy as jnp
        import numpy as np
        BSZ, L, H, P = (8, 1024, 128, 64)
        DT_MIN, DT_MAX = (0.001, 0.1)

        def _binop(q_i, q_j):
            A_i, b_i = q_i
            A_j, b_j = q_j
            return (A_j * A_i, A_j * b_i + b_j)
        Lambda = (Lambda_re + 1j * Lambda_im).astype(jnp.complex64)
        B_tilde = (B[..., 0] + 1j * B[..., 1]).astype(jnp.complex64)
        C_tilde = (C[..., 0] + 1j * C[..., 1]).astype(jnp.complex64)
        step = jnp.exp(log_step[:, 0])
        Lambda_bar = jnp.exp(Lambda * step)
        B_bar = ((Lambda_bar - 1.0) / Lambda)[:, None] * B_tilde
        Bu = jnp.einsum('blh,ph->blp', u, B_bar)
        Lam = jnp.broadcast_to(Lambda_bar, Bu.shape)
        _, xs = jax.lax.associative_scan(_binop, (Lam, Bu), axis=1)
        ys = 2.0 * jnp.einsum('blp,hp->blh', xs, C_tilde).real + D * u
        return jax.nn.gelu(ys)

    def _L0_ffn_ref(x, router_w, router_b, fc1_w, fc1_b, fc2_w, fc2_b):
        import jax, jax.numpy as jnp
        import numpy as np
        TOP_K = 2
        n_experts = router_w.shape[0]
        temp = 1.0
        logits = (jnp.einsum('btd,ed->bte', x, router_w) + router_b) / temp
        topk_val, topk_idx = jax.lax.top_k(logits, TOP_K)
        weights = jax.nn.softmax(topk_val, axis=-1)
        onehot = jax.nn.one_hot(topk_idx, n_experts, dtype=x.dtype)
        cw = jnp.einsum('btk,btke->bte', weights, onehot)
        h = jnp.einsum('btd,efd->btef', x, fc1_w) + fc1_b
        h1, h2 = jnp.split(h, 2, axis=-1)
        a = jax.nn.silu(h1) * h2
        y = jnp.einsum('bteh,edh->bted', a, fc2_w) + fc2_b
        out = jnp.einsum('bted,bte->btd', y, cw)
        return out
    h = _L0_tok_ref(x, L0_tok_W, L0_tok_b)
    h = h + _L0_attn_ref(_layernorm(h, axis=-1), L0_attn_Lambda_re, L0_attn_Lambda_im, L0_attn_B, L0_attn_C, L0_attn_D, L0_attn_log_step)
    h = h + _L0_ffn_ref(_layernorm(h, axis=-1), L0_ffn_router_w, L0_ffn_router_b, L0_ffn_fc1_w, L0_ffn_fc1_b, L0_ffn_fc2_w, L0_ffn_fc2_b)
    return h

_drawn_inputs = setup_inputs


def setup_inputs(seed=0):
    import zlib

    import numpy as np

    out = dict(_drawn_inputs(seed))
    spreads = {'L0_attn_Lambda_re': (-0.5, 0.6),
     'L0_ffn_router_b': (0.0, 0.279),
     'L0_ffn_fc1_b': (0.0, 0.8),
     'L0_ffn_fc2_b': (0.0, 0.573)}
    factors = {'L0_ffn_fc1_w': 8.0, 'L0_ffn_fc2_w': 8.0}
    for name, (base, spread) in spreads.items():
        noise = np.random.default_rng([zlib.crc32(name.encode()), seed]).standard_normal(out[name].shape)
        drawn = base * np.exp(spread * noise) if base else spread * noise
        out[name] = jnp.asarray(drawn.astype(out[name].dtype))
    for name, factor in factors.items():
        out[name] = (out[name] * factor).astype(out[name].dtype)
    return out
```

```python
from contextlib import ExitStack

import numpy as np

import concourse.bass as bass
from concourse import mybir

F32 = mybir.dt.float32
BF16 = mybir.dt.bfloat16
I32 = mybir.dt.int32
U32 = mybir.dt.uint32
ALU = mybir.AluOpType
ACT = mybir.ActivationFunctionType
AX = mybir.AxisListType

P = 128
D = 128
SEQ = 256
NT = 16
GT = 4
NG = NT // GT
GW = GT * P
TOKENS = NT * P
NE = 8
K = 2
HID = 256
ROW = D + 1
REGION = TOKENS + P
PAD_REGION = NE * REGION
NTILES = -(-(TOKENS * K // P + NE - 1) // 4) * 4
BODY = 4
SKIP = 1 << 20
EPS = 1e-5
MAGIC = 1.5 * 2.0 ** 23
LN2_HI, LN2_LO = 0.693359375, -2.12194440e-4
PI = 3.141592653589793
TWO_PI_1 = 6.28125
TWO_PI_2 = 2028.0 / 2 ** 20
TWO_PI_3 = 2 * PI - TWO_PI_1 - TWO_PI_2
EXP_TAYLOR = [1 / 5040, 1 / 720, 1 / 120, 1 / 24, 1 / 6, 1 / 2]


def lm_tower(nc, tok, emb_table, emb_b, pos, lam_re, lam_im, log_step, b_mat, c_mat, d_vec,
             router_w, router_b, w1, b12, w2, out):
    with ExitStack() as ctx:
        def sb(name, shape, dt=F32):
            return ctx.enter_context(nc.sbuf_tensor(name, shape, dt))

        def bank(name, shape=(P, 512), dt=F32):
            return ctx.enter_context(nc.psum_tensor(name, list(shape), dt))

        def sem(name):
            return ctx.enter_context(nc.semaphore(name))

        sorted_rows = nc.dram_tensor("sorted_rows", [PAD_REGION + P, ROW], F32)
        results = nc.dram_tensor("results", [K * TOKENS, D], F32)

        tok_sb = sb("tok_sb", [P, NT], I32)
        pos_sb = sb("pos_sb", [P, 2, D])
        embb_sb = sb("embb_sb", [P, D])
        prm = sb("prm", [P, 4])
        bm = sb("bm", [P, 2, D])
        cm = sb("cm", [P, 2, D])
        rw_sb = sb("rw_sb", [P, NE])
        rb_sb = sb("rb_sb", [P, GT, NE])
        w1_sb = sb("w1_sb", [P, NE * 2 * HID])
        w2_sb = sb("w2_sb", [P, NE * 2 * D])
        bias_f = sb("bias_f", [40, P])
        bias_r = sb("bias_r", [40, P])
        bias_p = sb("bias_p", [40, 3, P], BF16)
        bias3 = sb("bias3", [3, 40 * P], BF16)
        ones3 = sb("ones3", [3, P], BF16)
        ident = sb("ident", [P, P])
        ones_b = sb("ones_b", [P, P], BF16)
        before = sb("before", [P, P], BF16)
        half = sb("half", [P, 2])
        iota_e = sb("iota_e", [P, GT, NE])
        base_e = sb("base_e", [P, GT, NE])
        iota_t = sb("iota_t", [1, NTILES])
        pad = sb("pad", [P, ROW])

        col = sb("col", [P, 40])
        cosw = sb("cosw", [P, SEQ + 1])
        sinw = sb("sinw", [P, SEQ + 1])
        wtmp = sb("wtmp", [P, 2, SEQ + 1])
        decay = sb("decay", [P, SEQ])
        bbar = sb("bbar", [P, 2, D])
        bbarT = sb("bbarT", [P, 2, P])
        cmat = sb("cmat", [P, 2, D])
        diag = sb("diag", [P, P])

        res = sb("res", [P, NT, D])
        stats = sb("stats", [P, GT, 6])
        mv = sb("mv", [P, 2, 2, GT, 2])
        nwt = sb("nwt", [P, 4, GT])
        nwi = sb("nwi", [P, GT], I32)
        rstd = sb("rstd", [P, 2, 2, GT])
        nmr = sb("nmr", [P, 2, 2, GT])
        un = sb("un", [P, GT, D])
        uT = sb("uT", [P, 2, GW])
        rot = sb("rot", [P, 2, GW])
        zin = sb("zin", [P, GW])
        zst = sb("zst", [P, GW])
        zrot = sb("zrot", [P, 2, GW])
        gel = sb("gel", [P, GW])
        rows = sb("rows", [P, K, NT, ROW])
        xnT = sb("xnT", [P, GW])
        logit = sb("logit", [P, GT, NE])
        top8 = sb("top8", [P, NT, 8])
        arg8 = sb("arg8", [P, GT, 8], U32)
        argf = sb("argf", [P, GT, K])
        pick = sb("pick", [P, K, GT, NE])
        picked = sb("picked", [P, GT, NE], BF16)
        seen = sb("seen", [P, NT + 1, NE], BF16)
        place = sb("place", [P, GT, NE])
        ptmp = sb("ptmp", [P, K, GT, NE])
        slot = sb("slot", [P, K, NT], I32)
        wdiff = sb("wdiff", [P, NT])
        wgt = sb("wgt", [P, K, NT])

        cnt_i = sb("cnt_i", [1, 2, NE], I32)
        cnt_f = sb("cnt_f", [1, 4, NE])
        over = sb("over", [1, 2, NTILES, NE])
        tile_e = sb("tile_e", [1, 2, NTILES])
        tile_ei = sb("tile_ei", [1, NTILES], I32)
        tile_ri = sb("tile_ri", [1, NTILES], I32)
        pad_ri = sb("pad_ri", [1, NE], I32)

        xt = [sb(f"xt{j}", [P, ROW]) for j in range(BODY)]
        xT = [sb(f"xT{j}", [P, P]) for j in range(2)]
        sil = [sb(f"sil{j}", [P, HID]) for j in range(2)]
        act_h = [sb(f"act_h{j}", [P, HID]) for j in range(2)]
        aT = [sb(f"aT{j}", [P, 2 * P]) for j in range(2)]
        ysb = [sb(f"ysb{j}", [P, D]) for j in range(BODY)]
        yres = sb("yres", [P, K, NT, D])

        banks = [bank(f"bank{i}") for i in range(8)]
        ps_uT, ps_v, ps_vs, ps_y, ps_xT, ps_lg, ps_pos, ps_set = banks
        ps_t = banks[0:2]
        ps_h = banks[2:4]
        ps_a = banks[4:6]
        ps_o = banks[6:8]

        s_tok = sem("s_tok"); s_small = sem("s_small"); s_prm = sem("s_prm"); s_w = sem("s_w")
        s_const = sem("s_const"); s_ident = sem("s_ident"); s_pool = sem("s_pool")
        s_dve = sem("s_dve"); s_act = sem("s_act")
        s_gath = [sem(f"s_gath{g}") for g in range(NG)]
        s_theta = sem("s_theta"); s_trig = sem("s_trig"); s_bbar = sem("s_bbar")
        s_bbarTp = sem("s_bbarTp"); s_bbarT = sem("s_bbarT"); s_cmat = sem("s_cmat")
        s_biasp = sem("s_biasp"); s_bias = sem("s_bias")
        s_n1 = sem("s_n1"); s_un = sem("s_un"); s_uTp = sem("s_uTp"); s_uT = sem("s_uT")
        s_bu = sem("s_bu"); s_rotin = sem("s_rotin"); s_zrot = sem("s_zrot"); s_y = sem("s_y")
        s_gel = sem("s_gel"); s_n2 = sem("s_n2"); s_xn = sem("s_xn"); s_rows = sem("s_rows")
        s_xTp = sem("s_xTp"); s_xnT = sem("s_xnT"); s_lg = sem("s_lg"); s_picked = sem("s_picked")
        s_pos = sem("s_pos"); s_slot = sem("s_slot"); s_scat = sem("s_scat")
        s_cnt = sem("s_cnt"); s_table = sem("s_table"); s_pads = sem("s_pads")
        s_wd = sem("s_wd"); s_wgt = sem("s_wgt")
        s_xt = [sem(f"s_xt{j}") for j in range(BODY)]
        s_tp = sem("s_tp"); s_te = sem("s_te"); s_hp = sem("s_hp"); s_sil = sem("s_sil")
        s_a = sem("s_a"); s_ap = sem("s_ap"); s_ae = sem("s_ae"); s_op = sem("s_op"); s_oe = sem("s_oe")
        s_ys = [sem(f"s_ys{j}") for j in range(BODY)]
        s_loading = sem("s_loading"); s_sending = sem("s_sending")
        s_yl = [sem(f"s_yl{g}") for g in range(NG)]; s_fin = sem("s_fin"); s_out = sem("s_out")

        block = ctx.enter_context(nc.Block())

        def wait_free(eng, semaphore, count):
            if not isinstance(count, int) or count > 0:
                eng.wait_ge(semaphore, count)

        def run_steps(eng, step, first, last):
            for s in range(first, BODY):
                step(s, s % BODY)
            with eng.Fori(1, NTILES // BODY - 1) as i:
                for j in range(BODY):
                    step(i * BODY + j, j)
            for s in range(NTILES - BODY, last):
                step(s, s % BODY)

        @block.sync
        def _(sp):
            sp.dma_start(tok_sb[:, :], tok).then_inc(s_tok, 16)
            for h in range(2):
                q = slice(64 * h, 64 * h + 64)
                sp.dma_start(prm[q, 0:1], lam_re).then_inc(s_prm, 16)
                sp.dma_start(prm[q, 1:2], lam_im).then_inc(s_prm, 16)
                sp.dma_start(prm[q, 2:3], log_step).then_inc(s_prm, 16)
            sp.dma_start(prm[:, 3:4], d_vec).then_inc(s_prm, 16)
            sp.dma_start(pos_sb[:, :, :], pos).then_inc(s_small, 16)
            sp.dma_start(embb_sb[:, :], emb_b.partition_broadcast(P)).then_inc(s_small, 16)
            for h in range(2):
                q = slice(64 * h, 64 * h + 64)
                for c in range(2):
                    sp.dma_start(bm[q, c, :], b_mat[c]).then_inc(s_small, 16)
                    sp.dma_start(cm[q, c, :], c_mat[c if h == 0 else 1 - c]).then_inc(s_small, 16)
            sp.dma_start(rw_sb[:, :], router_w).then_inc(s_small, 16)
            for j in range(GT):
                sp.dma_start(rb_sb[:, j, :], router_b.partition_broadcast(P)).then_inc(s_small, 16)
            sp.dma_start(bias_f[:, :], b12).then_inc(s_small, 16)
            sp.dma_start(w1_sb[:, :], w1).then_inc(s_w, 16)
            sp.dma_start(w2_sb[:, :], w2).then_inc(s_w, 16)
            sp.wait_ge(s_biasp, 1)
            for k in range(3):
                sp.dma_start(bias3[k:k + 1, :].rearrange("o (a b) -> o a b", a=40),
                             bias_p[:, k, :]).then_inc(s_bias, 16)
            sp.wait_ge(s_const, 2)
            sp.dma_start(sorted_rows[PAD_REGION:PAD_REGION + P, :], pad[:, :]).then_inc(s_pads, 16)
            sp.wait_ge(s_table, 1)
            for e in range(NE):
                r = sp.value_load(pad_ri[0:1, e:e + 1], min_val=0, max_val=PAD_REGION - P)
                sp.dma_start(sorted_rows[bass.ds(r, P), :], pad[:, :]).then_inc(s_pads, 16)
            sp.wait_ge(s_pads, 16 * (NE + 1))
            sp.wait_ge(s_scat, 16 * K * NT)

            for j in range(BODY):
                r = sp.value_load(tile_ri[0:1, j:j + 1], min_val=0, max_val=PAD_REGION)
                sp.dma_start(xt[j][:, :], sorted_rows[bass.ds(r, P), :]).then_inc(s_xt[j], 16)
            with sp.Fori(1, NTILES // BODY) as i:
                for j in range(BODY):
                    r = sp.value_load(tile_ri[0:1, bass.ds(i * BODY + j, 1)], min_val=0, max_val=PAD_REGION)
                    sp.wait_ge(s_tp, i * BODY + (j - BODY + 1))
                    sp.sem_inc(s_loading, 1)
                    sp.wait_ge(s_ys[j], i * 16)
                    sp.sem_inc(s_loading, 1)
                    sp.dma_start(xt[j][:, :], sorted_rows[bass.ds(r, P), :]).then_inc(s_xt[j], 16)

            for j in range(BODY):
                sp.wait_ge(s_ys[j], 16 * (NTILES // BODY))
            for g in range(NG):
                for k in range(K):
                    lo = k * TOKENS + g * GW
                    sp.dma_start(yres[:, k, GT * g:GT * g + GT, :],
                                 results[lo:lo + GW, :].rearrange("(t p) d -> p t d", p=P)
                                 ).then_inc(s_yl[g], 16)
            out_rows = out.rearrange("b s d -> (b s) d")
            for g in range(NG):
                sp.wait_ge(s_fin, g + 1)
                sp.dma_start(out_rows[g * GW:g * GW + GW, :].rearrange("(t p) d -> p t d", p=P),
                             res[:, GT * g:GT * g + GT, :]).then_inc(s_out, 16)
            sp.wait_ge(s_out, 16 * NG)

        @block.gpsimd
        def _(pool):
            pool.wait_ge(s_tok, 16)
            gp = nc.gpsimd

            def gather(g):
                for j in range(GT):
                    t = GT * g + j
                    gp.indirect_dma_start(res[:, t, :], None, emb_table,
                                          bass.IndirectOffsetOnAxis(ap=tok_sb[:, t:t + 1], axis=0)
                                          ).then_inc(s_gath[g], 16)

            gather(0)
            gp.memset(ident[:, :], 0.0).then_inc(s_pool, 1)
            pool.wait_ge(s_pool, 1)
            gp.affine_select(out=ident[:, :], in_=ident[:, :], compare_op=ALU.not_equal, fill=1.0, base=0,
                             pattern=[[-1, P]], channel_multiplier=1).then_inc(s_ident, 1)
            gp.memset(half[:, :], 0.0).then_inc(s_pool, 1)
            pool.wait_ge(s_pool, 2)
            gp.memset(half[0:64, 0:1], 1.0).then_inc(s_ident, 1)
            gp.memset(half[64:P, 1:2], 1.0).then_inc(s_ident, 1)
            gather(1)
            pool.wait_ge(s_ident, 3)
            gp.memset(ones_b[:, :], 1.0).then_inc(s_pool, 1)
            pool.wait_ge(s_pool, 3)
            gp.affine_select(out=before[:, :], in_=ones_b[:, :], compare_op=ALU.is_gt, fill=0.0, base=0,
                             pattern=[[1, P]], channel_multiplier=-1).then_inc(s_pool, 1)
            gp.memset(ones3[:, :], 1.0).then_inc(s_pool, 1)
            gp.memset(seen[:, 0, :], 0.0).then_inc(s_pool, 1)
            gp.iota(iota_e[:, :, :], [[0, GT], [1, NE]], base=0, channel_multiplier=0,
                    allow_small_or_imprecise_dtypes=True).then_inc(s_pool, 1)
            gp.iota(base_e[:, :, :], [[0, GT], [REGION, NE]], base=0, channel_multiplier=0,
                    allow_small_or_imprecise_dtypes=True).then_inc(s_pool, 1)
            gp.iota(iota_t[:, :], [[1, NTILES]], base=0, channel_multiplier=0,
                    allow_small_or_imprecise_dtypes=True).then_inc(s_pool, 1)
            pool.wait_ge(s_pool, 9)
            gp.iota(rows[:, :, :, D:ROW].bitcast(I32), [[TOKENS, K], [P, NT], [0, 1]], base=0,
                    channel_multiplier=1).then_inc(s_const, 1)
            gp.memset(pad[:, 0:D], 0.0).then_inc(s_pool, 1)
            pool.wait_ge(s_pool, 10)
            gp.memset(pad[:, D:ROW].bitcast(I32), SKIP).then_inc(s_const, 1)
            gather(2)
            gather(3)
            for g in range(NG):
                pool.wait_ge(s_slot, g + 1)
                pool.wait_ge(s_rows, g + 1)
                for j in range(GT):
                    for k in range(K):
                        t = GT * g + j
                        gp.indirect_dma_start(sorted_rows[:, :],
                                              bass.IndirectOffsetOnAxis(ap=slot[:, k, t:t + 1], axis=0),
                                              rows[:, k, t, :], None).then_inc(s_scat, 16)

            bound = pool.alloc_register("last_result")
            pool.reg_mov(bound, K * TOKENS - 1)

            def scatter(t, j):
                pool.wait_ge(s_oe, t + 1)
                pool.sem_inc(s_sending, 1)
                gp.indirect_dma_start(results[:, :],
                                      bass.IndirectOffsetOnAxis(ap=xt[j][:, D:ROW].bitcast(I32), axis=0),
                                      ysb[j][:, :], None, bounds_check=bound, oob_is_err=False
                                      ).then_inc(s_ys[j], 16)
            run_steps(pool, scatter, 0, NTILES)

        @block.vector
        def _(dve):
            v = nc.vector
            n = [0]

            def step(ins):
                ins.then_inc(s_dve, 1)
                n[0] += 1
                dve.wait_ge(s_dve, n[0])

            def C(i):
                return col[:, i:i + 1]

            def exp_col(dst, src, t):
                nn, f, p, pw = t, t + 1, t + 2, t + 3
                step(v.tensor_scalar(C(nn), src, 1.4426950408889634, MAGIC, ALU.mult, ALU.add))
                step(v.tensor_scalar(C(nn), C(nn), MAGIC, -126.0, ALU.subtract, ALU.max))
                step(v.scalar_tensor_tensor(C(f), C(nn), -LN2_HI, src, ALU.mult, ALU.add))
                step(v.scalar_tensor_tensor(C(f), C(nn), -LN2_LO, C(f), ALU.mult, ALU.add))
                step(v.tensor_scalar(C(pw).bitcast(I32), C(nn), 127.0, 8388608.0, ALU.add, ALU.mult))
                step(v.tensor_scalar(C(p), C(f), EXP_TAYLOR[0], None, ALU.mult))
                for c in EXP_TAYLOR[1:] + [1.0]:
                    step(v.scalar_tensor_tensor(C(p), C(p), c, C(f), ALU.add, ALU.mult))
                step(v.scalar_tensor_tensor(dst, C(p), 1.0, C(pw), ALU.add, ALU.mult))

            dve.wait_ge(s_prm, 16 * 7)
            LR, LI, LS, DV = (prm[:, i:i + 1] for i in range(4))
            STEP, RM, TH, KT, COS, SIN, ARG, T0, T1, NR, NI, DEN, FR, FI, CA, CB, NCB = range(4, 21)
            exp_col(C(STEP), LS, 0)
            step(v.tensor_tensor(C(TH), LI, C(STEP), ALU.mult))
            step(v.tensor_scalar(C(KT), C(TH), 1 / (2 * PI), MAGIC, ALU.mult, ALU.add))
            step(v.tensor_scalar(C(KT), C(KT), MAGIC, None, ALU.subtract))
            step(v.scalar_tensor_tensor(C(TH), C(KT), -TWO_PI_1, C(TH), ALU.mult, ALU.add))
            step(v.scalar_tensor_tensor(C(TH), C(KT), -TWO_PI_2, C(TH), ALU.mult, ALU.add))
            step(v.scalar_tensor_tensor(C(TH), C(KT), -TWO_PI_3, C(TH), ALU.mult, ALU.add))
            step(v.tensor_scalar(C(TH), C(TH), 3.1415925, -3.1415925, ALU.min, ALU.max))
            step(v.tensor_scalar(C(T0), C(TH), -1.0, None, ALU.mult))
            step(v.tensor_tensor(C(T0), C(T0), C(TH), ALU.max))
            v.tensor_scalar(C(ARG), C(T0), -1.0, PI / 2, ALU.mult, ALU.add).then_inc(s_theta, 1)
            step(v.tensor_tensor(C(T1), LR, C(STEP), ALU.mult))
            exp_col(C(RM), C(T1), 0)
            step(v.tensor_scalar(decay[:, :], decay_zero(v, decay, step), C(RM), None, ALU.add))
            dve.wait_ge(s_trig, 2)
            step(v.tensor_tensor(C(NR), C(RM), C(COS), ALU.mult))
            step(v.tensor_scalar(C(NR), C(NR), -1.0, None, ALU.add))
            step(v.tensor_tensor(C(NI), C(RM), C(SIN), ALU.mult))
            step(v.tensor_tensor(C(DEN), LR, LR, ALU.mult))
            step(v.scalar_tensor_tensor(C(DEN), LI, LI, C(DEN), ALU.mult, ALU.add))
            step(v.reciprocal(C(DEN), C(DEN)))
            step(v.tensor_tensor(C(T0), C(NI), LI, ALU.mult))
            step(v.scalar_tensor_tensor(C(FR), C(NR), LR, C(T0), ALU.mult, ALU.add))
            step(v.tensor_tensor(C(FR), C(FR), C(DEN), ALU.mult))
            step(v.tensor_tensor(C(T0), C(NR), LI, ALU.mult))
            step(v.scalar_tensor_tensor(C(FI), C(NI), LR, C(T0), ALU.mult, ALU.subtract))
            step(v.tensor_tensor(C(FI), C(FI), C(DEN), ALU.mult))
            dve.wait_ge(s_ident, 3)
            step(v.tensor_tensor(C(T0), C(FI), half[:, 1:2], ALU.mult))
            step(v.scalar_tensor_tensor(C(CA), C(FR), half[:, 0:1], C(T0), ALU.mult, ALU.add))
            step(v.tensor_tensor(C(T0), C(FI), half[:, 0:1], ALU.mult))
            step(v.scalar_tensor_tensor(C(CB), C(FR), half[:, 1:2], C(T0), ALU.mult, ALU.subtract))
            step(v.tensor_scalar(C(NCB), C(CB), -1.0, None, ALU.mult))
            dve.wait_ge(s_small, 16 * 16)
            step(v.tensor_scalar(bbar[:, 0, :], bm[:, 1, :], C(CB), None, ALU.mult))
            step(v.scalar_tensor_tensor(bbar[:, 0, :], bm[:, 0, :], C(CA), bbar[:, 0, :], ALU.mult, ALU.add))
            step(v.tensor_scalar(bbar[:, 1, :], bm[:, 1, :], C(CA), None, ALU.mult))
            v.scalar_tensor_tensor(bbar[:, 1, :], bm[:, 0, :], C(NCB), bbar[:, 1, :],
                                   ALU.mult, ALU.add).then_inc(s_bbar, 1)
            step(v.tensor_scalar(C(T0), half[:, 0:1], 4.0, -2.0, ALU.mult, ALU.add))
            step(v.tensor_scalar(cmat[:, 0, :], cm[:, 0, :], C(T0), None, ALU.mult))
            step(v.tensor_scalar(cmat[:, 1, :], cm[:, 1, :], -2.0, None, ALU.mult))
            v.tensor_scalar(diag[:, :], ident[:, :], DV, None, ALU.mult).then_inc(s_cmat, 1)
            step(v.memset(cosw[:, 0:1], 1.0))
            step(v.memset(sinw[:, 0:1], 0.0))
            step(v.tensor_copy(cosw[:, 1:2], C(COS)))
            step(v.tensor_copy(sinw[:, 1:2], C(SIN)))
            m = 1
            while m < SEQ:
                cj, sj = cosw[:, 1:m + 1], sinw[:, 1:m + 1]
                cmm, smm = cosw[:, m:m + 1], sinw[:, m:m + 1]
                step(v.tensor_scalar(wtmp[:, 0, 0:m], sj, smm, None, ALU.mult))
                step(v.tensor_scalar(wtmp[:, 1, 0:m], cj, smm, None, ALU.mult))
                v.scalar_tensor_tensor(cosw[:, m + 1:2 * m + 1], cj, cmm, wtmp[:, 0, 0:m],
                                       ALU.mult, ALU.subtract).then_inc(s_dve, 1)
                n[0] += 1
                step(v.scalar_tensor_tensor(sinw[:, m + 1:2 * m + 1], sj, cmm, wtmp[:, 1, 0:m],
                                            ALU.mult, ALU.add))
                m *= 2
            step(v.tensor_tensor(wtmp[:, 0, :], cosw[:, :], cosw[:, :], ALU.mult))
            step(v.tensor_tensor(wtmp[:, 1, :], sinw[:, :], sinw[:, :], ALU.mult))
            step(v.tensor_tensor(wtmp[:, 0, :], wtmp[:, 0, :], wtmp[:, 1, :], ALU.add))
            step(v.tensor_scalar(wtmp[:, 0, :], wtmp[:, 0, :], -0.5, 1.5, ALU.mult, ALU.add))
            step(v.tensor_tensor(cosw[:, :], cosw[:, :], wtmp[:, 0, :], ALU.mult))
            step(v.tensor_tensor(sinw[:, :], sinw[:, :], wtmp[:, 0, :], ALU.mult))
            step(v.tensor_copy(bias_p[:, 0, :], bias_f[:, :]))
            step(v.tensor_tensor(bias_r[:, :], bias_f[:, :], bias_p[:, 0, :], ALU.subtract))
            step(v.tensor_copy(bias_p[:, 1, :], bias_r[:, :]))
            step(v.tensor_tensor(bias_r[:, :], bias_r[:, :], bias_p[:, 1, :], ALU.subtract))
            v.tensor_copy(bias_p[:, 2, :], bias_r[:, :]).then_inc(s_biasp, 1)
            for h in range(2):
                step(v.tensor_tensor(pos_sb[:, h, :], pos_sb[:, h, :], embb_sb[:, :], ALU.add))

            def norm_scalars(which, g, done):
                st = mv[:, which, g % 2]
                for j in range(GT):
                    v.bn_stats(stats[:, j, :], res[:, GT * g + j, :]).then_inc(s_dve, 1)
                n[0] += GT
                dve.wait_ge(s_dve, n[0])
                for j in range(GT):
                    v.bn_aggr(st[:, j, :], stats[:, j, :]).then_inc(s_dve, 1)
                n[0] += GT
                dve.wait_ge(s_dve, n[0])
                var, y, a = nwt[:, 0, :], nwt[:, 1, :], nwt[:, 2, :]
                step(v.tensor_scalar(var, st[:, :, 1], EPS, None, ALU.add))
                step(v.tensor_scalar(nwi[:, :], var.bitcast(I32), 1, None, ALU.arith_shift_right))
                step(v.tensor_scalar(y.bitcast(I32), nwi[:, :], -1.0, float(0x5F3759DF), ALU.mult, ALU.add))
                r = rstd[:, which, g % 2, :]
                for k in range(3):
                    step(v.tensor_tensor(a, y, y, ALU.mult))
                    step(v.scalar_tensor_tensor(a, a, -0.5, var, ALU.mult, ALU.mult))
                    o = r if k == 2 else y
                    step(v.scalar_tensor_tensor(o, a, 1.5, y, ALU.add, ALU.mult))
                v.scalar_tensor_tensor(nmr[:, which, g % 2, :], st[:, :, 0], -1.0, r,
                                       ALU.mult, ALU.mult).then_inc(done, 1)

            def embed(g):
                dve.wait_ge(s_gath[g], 16 * GT)
                e = res[:, GT * g:GT * g + GT, :].rearrange("p (b h) d -> p b h d", h=2)
                step(v.tensor_tensor(e, e, pos_sb[:, None, :, :].to_broadcast([P, 2, 2, D]), ALU.add))
                if g >= 2:
                    dve.wait_ge(s_un, g - 1)
                norm_scalars(0, g, s_n1)

            def per_seq(ap):
                return ap.rearrange("p (b t) -> p b t", b=2)

            cos_b = cosw[:, None, 0:SEQ].to_broadcast([P, 2, SEQ])
            sin_b = sinw[:, None, 0:SEQ].to_broadcast([P, 2, SEQ])

            def scan(g):
                dve.wait_ge(s_bu, g + 1)
                v.tensor_tensor(per_seq(rot[:, 0, :]), per_seq(ps_v[:, :]), cos_b, ALU.mult).then_inc(s_dve, 1)
                v.tensor_tensor(per_seq(rot[:, 1, :]), per_seq(ps_vs[:, :]), sin_b, ALU.mult).then_inc(s_rotin, 1)
                n[0] += 1
                dve.wait_ge(s_dve, n[0])
                dve.wait_ge(s_rotin, g + 1)
                step(v.tensor_tensor(zin[:, :], rot[:, 0, :], rot[:, 1, :], ALU.add))
                for b in range(2):
                    q = slice(SEQ * b, SEQ * b + SEQ)
                    v.tensor_tensor_scan(zst[:, q], decay[:, :], zin[:, q], 0.0, ALU.mult, ALU.add).then_inc(s_dve, 1)
                n[0] += 2
                dve.wait_ge(s_dve, n[0])
                if g >= 1:
                    dve.wait_ge(s_y, g)
                v.tensor_tensor(per_seq(zrot[:, 0, :]), per_seq(zst[:, :]), cos_b, ALU.mult).then_inc(s_zrot, 1)
                v.tensor_tensor(per_seq(zrot[:, 1, :]), per_seq(zst[:, :]), sin_b, ALU.mult).then_inc(s_zrot, 1)

            def add_gelu(g):
                dve.wait_ge(s_gel, g + 1)
                e = res[:, GT * g:GT * g + GT, :].rearrange("p j d -> p (j d)")
                step(v.tensor_tensor(e, e, gel[:, :], ALU.add))
                if g >= 2:
                    dve.wait_ge(s_xn, g - 1)
                norm_scalars(1, g, s_n2)

            def choose(g):
                dve.wait_ge(s_lg, g + 1)
                step(v.tensor_tensor(logit[:, :, :], ps_lg[:, 0:GT * NE].rearrange("p (j e) -> p j e", e=NE),
                                     rb_sb[:, :, :], ALU.add))
                top = top8[:, GT * g:GT * g + GT, :]
                for j in range(GT):
                    v.max(top[:, j, :], logit[:, j, :]).then_inc(s_dve, 1)
                n[0] += GT
                dve.wait_ge(s_dve, n[0])
                for j in range(GT):
                    v.max_index(arg8[:, j, :], top[:, j, :], logit[:, j, :]).then_inc(s_dve, 1)
                n[0] += GT
                dve.wait_ge(s_dve, n[0])
                step(v.tensor_copy(argf[:, :, :], arg8[:, :, 0:K]))
                for k in range(K):
                    v.tensor_tensor(pick[:, k], iota_e[:, :, :], argf[:, :, k:k + 1].to_broadcast([P, GT, NE]),
                                    ALU.is_equal).then_inc(s_dve, 1)
                n[0] += K
                dve.wait_ge(s_dve, n[0])
                if g >= 1:
                    dve.wait_ge(s_pos, g)
                step(v.tensor_tensor(picked[:, :, :], pick[:, 0], pick[:, 1], ALU.add))
                for j in range(GT):
                    t = GT * g + j
                    ins = v.tensor_tensor(seen[:, t + 1, :], seen[:, t, :], picked[:, j, :], ALU.add)
                    if j < GT - 1:
                        step(ins)
                    else:
                        ins.then_inc(s_picked, 1)
                dve.wait_ge(s_picked, g + 1)

            def find_slots(g):
                dve.wait_ge(s_pos, g + 1)
                step(v.tensor_tensor(place[:, :, :], ps_pos[:, 0:GT * NE].rearrange("p (j e) -> p j e", e=NE),
                                     base_e[:, :, :], ALU.add))
                for k in range(K):
                    v.tensor_tensor(ptmp[:, k], place[:, :, :], pick[:, k], ALU.mult).then_inc(s_dve, 1)
                n[0] += K
                dve.wait_ge(s_dve, n[0])
                for k in range(K):
                    with nc.allow_low_precision(reason="row numbers are exact integers"):
                        ins = v.tensor_reduce(slot[:, k, GT * g:GT * g + GT], ptmp[:, k], AX.X, ALU.add)
                    if k == K - 1:
                        ins.then_inc(s_slot, 1)
                    else:
                        step(ins)
                dve.wait_ge(s_slot, g + 1)

            dve.wait_ge(s_const, 1)
            embed(0)
            embed(1)
            scan(0)
            embed(2)
            add_gelu(0)
            scan(1)
            choose(0)
            find_slots(0)
            embed(3)
            add_gelu(1)
            scan(2)
            choose(1)
            find_slots(1)
            add_gelu(2)
            scan(3)
            choose(2)
            find_slots(2)
            add_gelu(3)
            choose(3)
            find_slots(3)

            dve.wait_ge(s_cnt, 1)
            count, tiles, ends, delta = (cnt_f[:, i, :] for i in range(4))
            step(v.tensor_copy(count, ps_set[0:1, 0:NE]))
            step(v.tensor_scalar(cnt_i[:, 0, :], count, float(P - 1), None, ALU.add))
            step(v.tensor_scalar(cnt_i[:, 1, :], cnt_i[:, 0, :], 7, None, ALU.arith_shift_right))
            step(v.tensor_copy(tiles, cnt_i[:, 1, :]))
            step(v.tensor_tensor(pad_ri[:, :], count, base_e[0:1, 0, :], ALU.add))
            step(v.tensor_tensor_scan(ends, ones_like(v, step, over), tiles, 0.0, ALU.mult, ALU.add))
            step(v.tensor_scalar(delta, tiles, -float(P), float(REGION), ALU.mult, ALU.add))
            shape = [1, NTILES, NE]
            step(v.tensor_tensor(over[:, 0], iota_t[:, :, None].to_broadcast(shape),
                                 ends[:, None, :].to_broadcast(shape), ALU.is_ge))
            step(v.tensor_tensor(over[:, 1], over[:, 0], delta[:, None, :].to_broadcast(shape), ALU.mult))
            step(v.tensor_reduce(tile_e[:, 0, :], over[:, 0], AX.X, ALU.add))
            step(v.tensor_reduce(tile_e[:, 1, :], over[:, 1], AX.X, ALU.add))
            step(v.tensor_scalar(tile_ei[:, :], tile_e[:, 0, :], float(NE - 1), None, ALU.min))
            step(v.scalar_tensor_tensor(tile_e[:, 1, :], iota_t[:, :], float(P), tile_e[:, 1, :],
                                        ALU.mult, ALU.add))
            v.tensor_scalar(tile_ri[:, :], tile_e[:, 1, :], float(PAD_REGION), None, ALU.min).then_inc(s_table, 1)
            step(v.tensor_tensor(wdiff[:, :], top8[:, :, 0], top8[:, :, 1], ALU.subtract))
            v.tensor_scalar(wdiff[:, :], wdiff[:, :], 0.5, None, ALU.mult).then_inc(s_wd, 1)
            dve.wait_ge(s_wgt, 1)
            step(v.tensor_scalar(wgt[:, 0, :], wdiff[:, :], 0.5, 0.5, ALU.mult, ALU.add))
            step(v.tensor_scalar(wgt[:, 1, :], wdiff[:, :], -0.5, 0.5, ALU.mult, ALU.add))

            def work(s, j):
                static = isinstance(s, int)
                if not static or 0 <= s - 1 < NTILES:
                    t = s - 1
                    dve.wait_ge(s_ap, t + 1)
                    wait_free(dve, s_op, t - 1)
                    v.tensor_copy(aT[(j - 1) % 2][:, :], ps_a[(j - 1) % 2][:, 0:HID]).then_inc(s_ae, 1)
                if not static or s < NTILES:
                    dve.wait_ge(s_sil, s + 1)
                    wait_free(dve, s_ap, s - 1)
                    v.tensor_tensor(act_h[j % 2][:, :], sil[j % 2][:, :], ps_h[j % 2][:, HID:2 * HID],
                                    ALU.mult).then_inc(s_a, 1)
                if not static or s - 2 >= 0:
                    t = s - 2
                    dve.wait_ge(s_op, t + 1)
                    if not static or t >= BODY:
                        dve.wait_ge(s_ys[(j - 2) % BODY], uses(s, j, 2))
                    v.tensor_copy(ysb[(j - 2) % BODY][:, :], ps_o[j % 2][:, 0:D]).then_inc(s_oe, 1)

            def uses(s, j, back):
                if isinstance(s, int):
                    return 16 * ((s - back) // BODY)
                return (s - j) * (16 // BODY) - (16 if j < back else 0)

            def work_steps():
                for s in range(0, BODY + 2):
                    work(s, s % BODY)
            work_steps()
            for s in range(BODY + 2, 2 * BODY):
                work(s, s % BODY)
            with dve.Fori(2, NTILES // BODY) as i:
                for j in range(BODY):
                    work(i * BODY + j, j)
            for s in range(NTILES, NTILES + 2):
                work(s, s % BODY)

            for g in range(NG):
                dve.wait_ge(s_yl[g], 32)
                for j in range(GT):
                    t = GT * g + j
                    step(v.scalar_tensor_tensor(res[:, t, :], yres[:, 0, t, :], wgt[:, 0, t:t + 1], res[:, t, :],
                                                ALU.mult, ALU.add))
                    ins = v.scalar_tensor_tensor(res[:, t, :], yres[:, 1, t, :], wgt[:, 1, t:t + 1], res[:, t, :],
                                                 ALU.mult, ALU.add)
                    if j == GT - 1:
                        ins.then_inc(s_fin, 1)
                    else:
                        step(ins)

        @block.scalar
        def _(act):
            a = nc.scalar
            act.wait_ge(s_theta, 1)
            a.activation(col[:, 9:10], col[:, 6:7], ACT.Sin).then_inc(s_trig, 1)
            a.activation(col[:, 8:9], col[:, 10:11], ACT.Sin).then_inc(s_trig, 1)
            act.wait_ge(s_bbarTp, 1)
            a.copy(bbarT[:, :, :].rearrange("p c s -> p (c s)"), ps_set[:, 0:2 * P]).then_inc(s_bbarT, 1)

            def normed_u(g):
                act.wait_ge(s_n1, g + 1)
                if g >= 1:
                    act.wait_ge(s_uTp, g)
                for j in range(GT):
                    a.activation(un[:, j, :], res[:, GT * g + j, :], ACT.Identity,
                                 bias=nmr[:, 0, g % 2, j:j + 1], scale=rstd[:, 0, g % 2, j:j + 1]
                                 ).then_inc(s_un if j == GT - 1 else s_act, 1)

            def copy_uT(g):
                act.wait_ge(s_uTp, g + 1)
                if g >= 2:
                    act.wait_ge(s_y, g - 1)
                a.copy(uT[:, g % 2, :], ps_uT[:, :]).then_inc(s_uT, 1)

            def gelu(g):
                act.wait_ge(s_y, g + 1)
                if g >= 1:
                    act.wait_ge(s_n2, g)
                a.activation(gel[:, :], ps_y[:, :], ACT.Gelu_apprx_tanh).then_inc(s_gel, 1)

            def normed_x(g):
                act.wait_ge(s_n2, g + 1)
                for j in range(GT):
                    a.activation(rows[:, 0, GT * g + j, 0:D], res[:, GT * g + j, :], ACT.Identity,
                                 bias=nmr[:, 1, g % 2, j:j + 1], scale=rstd[:, 1, g % 2, j:j + 1]
                                 ).then_inc(s_xn if j == GT - 1 else s_act, 1)

            def copy_xnT(g):
                act.wait_ge(s_xTp, g + 1)
                if g >= 1:
                    act.wait_ge(s_lg, g)
                a.copy(xnT[:, :], ps_xT[:, :]).then_inc(s_xnT, 1)

            def second_rows(g):
                act.wait_ge(s_xn, g + 1)
                q = slice(GT * g, GT * g + GT)
                a.copy(rows[:, 1, q, 0:D], rows[:, 0, q, 0:D]).then_inc(s_rows, 1)

            normed_u(0); copy_uT(0)
            normed_u(1); copy_uT(1)
            gelu(0)
            normed_u(2); copy_uT(2)
            normed_x(0); copy_xnT(0); second_rows(0)
            gelu(1)
            normed_u(3); copy_uT(3)
            normed_x(1); copy_xnT(1); second_rows(1)
            gelu(2)
            normed_x(2); copy_xnT(2); second_rows(2)
            gelu(3)
            normed_x(3); copy_xnT(3); second_rows(3)
            act.wait_ge(s_wd, 1)
            a.activation(wdiff[:, :], wdiff[:, :], ACT.Tanh).then_inc(s_wgt, 1)

            def work(s, j):
                static = isinstance(s, int)
                if not static or s >= 0:
                    act.wait_ge(s_hp, s + 1)
                    wait_free(act, s_a, s - 1)
                    a.activation(sil[j % 2][:, :], ps_h[j % 2][:, 0:HID], ACT.Silu).then_inc(s_sil, 1)
                if not static or s + 1 < NTILES:
                    act.wait_ge(s_tp, s + 2)
                    wait_free(act, s_hp, s)
                    a.copy(xT[(j + 1) % 2][:, :], ps_t[(j + 1) % 2][:, 0:P]).then_inc(s_te, 1)
            run_steps(act, work, -1, NTILES)

        @block.tensor
        def _(pe):
            te = nc.tensor
            pe.wait_ge(s_ident, 3)
            pe.wait_ge(s_bbar, 1)
            te.transpose(ps_set[:, 0:P], bbar[:, 0, :], ident[:, :])
            te.transpose(ps_set[:, P:2 * P], bbar[:, 1, :], ident[:, :]).then_inc(s_bbarTp, 1)

            def turn_u(g):
                pe.wait_ge(s_un, g + 1)
                if g >= 1:
                    pe.wait_ge(s_uT, g)
                for j in range(GT):
                    ins = te.transpose(ps_uT[:, j * P:(j + 1) * P], un[:, j, :], ident[:, :])
                ins.then_inc(s_uTp, 1)

            def b_times_u(g):
                pe.wait_ge(s_uT, g + 1)
                if g == 0:
                    pe.wait_ge(s_bbarT, 1)
                else:
                    pe.wait_ge(s_rotin, g)
                te.matmul(ps_v[:, :], bbarT[:, 0, :], uT[:, g % 2, :], start=True, stop=True)
                te.matmul(ps_vs[:, :], bbarT[:, 1, :], uT[:, g % 2, :], start=True, stop=True).then_inc(s_bu, 1)

            def outputs(g):
                if g == 0:
                    pe.wait_ge(s_cmat, 1)
                else:
                    pe.wait_ge(s_gel, g)
                pe.wait_ge(s_zrot, 2 * g + 2)
                for j in range(GT):
                    q = slice(j * P, (j + 1) * P)
                    te.matmul(ps_y[:, q], zrot[:, 0, q], cmat[:, 0, :], start=True, stop=False)
                    te.matmul(ps_y[:, q], zrot[:, 1, q], cmat[:, 1, :], start=False, stop=False)
                    ins = te.matmul(ps_y[:, q], uT[:, g % 2, q], diag[:, :], start=False, stop=True)
                ins.then_inc(s_y, 1)

            def turn_x(g):
                pe.wait_ge(s_xn, g + 1)
                if g >= 1:
                    pe.wait_ge(s_xnT, g)
                for j in range(GT):
                    ins = te.transpose(ps_xT[:, j * P:(j + 1) * P], rows[:, 0, GT * g + j, 0:D], ident[:, :])
                ins.then_inc(s_xTp, 1)

            def logits(g):
                pe.wait_ge(s_xnT, g + 1)
                if g >= 1:
                    pe.wait_ge(s_picked, g)
                for j in range(GT):
                    ins = te.matmul(ps_lg[:, j * NE:(j + 1) * NE], xnT[:, j * P:(j + 1) * P], rw_sb[:, :],
                                    start=True, stop=True)
                ins.then_inc(s_lg, 1)

            def positions(g):
                pe.wait_ge(s_picked, g + 1)
                if g >= 1:
                    pe.wait_ge(s_slot, g)
                te.matmul(ps_pos[:, 0:GT * NE], before[:, :], picked[:, :, :].rearrange("p j e -> p (j e)"),
                          start=True, stop=False)
                te.matmul(ps_pos[:, 0:GT * NE], ones_b[:, :],
                          seen[:, GT * g:GT * g + GT, :].rearrange("p j e -> p (j e)"),
                          start=False, stop=True).then_inc(s_pos, 1)

            turn_u(0); b_times_u(0)
            turn_u(1)
            outputs(0)
            b_times_u(1)
            turn_u(2)
            turn_x(0); logits(0)
            outputs(1)
            b_times_u(2)
            positions(0)
            turn_u(3)
            turn_x(1); logits(1)
            outputs(2)
            b_times_u(3)
            positions(1)
            turn_x(2); logits(2)
            outputs(3)
            positions(2)
            turn_x(3); logits(3)
            positions(3)
            te.matmul(ps_set[:, 0:NE], ones_b[:, :], seen[:, NT, :], start=True, stop=True).then_inc(s_cnt, 1)

            pe.wait_ge(s_w, 32)
            pe.wait_ge(s_bias, 48)
            pe.wait_ge(s_table, 1)
            pe.wait_ge(s_slot, NG)

            def loads(s, j):
                if isinstance(s, int):
                    return 16 * ((s + 1) // BODY + 1)
                return (s - j) * (16 // BODY) + (32 if j == BODY - 1 else 16)

            def work(s, j):
                static = isinstance(s, int)
                if not static or 0 <= s < NTILES:
                    e = pe.value_load(tile_ei[0:1, bass.ds(s, 1)], min_val=0, max_val=NE - 1)
                    pe.wait_ge(s_te, s + 1)
                    wait_free(pe, s_a, s - 1)
                    te.matmul(ps_h[j % 2][:, :], xT[j % 2][:, :], w1_sb[:, bass.ds(e * (2 * HID), 2 * HID)],
                              start=True, stop=False)
                    te.matmul(ps_h[j % 2][:, :], ones3[:, :], bias3[:, bass.ds(e * (2 * HID), 2 * HID)],
                              start=False, stop=True).then_inc(s_hp, 1)
                if not static or 0 <= s - 1 < NTILES:
                    t = s - 1
                    pe.wait_ge(s_a, t + 1)
                    wait_free(pe, s_ae, t - 1)
                    b = (j - 1) % 2
                    te.transpose(ps_a[b][:, 0:P], act_h[b][:, 0:P], ident[:, :])
                    te.transpose(ps_a[b][:, P:2 * P], act_h[b][:, P:2 * P], ident[:, :]).then_inc(s_ap, 1)
                if not static or s + 1 < NTILES:
                    pe.wait_ge(s_xt[(j + 1) % BODY], loads(s, j))
                    wait_free(pe, s_te, s)
                    te.transpose(ps_t[(j + 1) % 2][:, 0:P], xt[(j + 1) % BODY][:, 0:D], ident[:, :]
                                 ).then_inc(s_tp, 1)
                if not static or s - 2 >= 0:
                    t = s - 2
                    e = pe.value_load(tile_ei[0:1, bass.ds(t, 1)], min_val=0, max_val=NE - 1)
                    pe.wait_ge(s_ae, t + 1)
                    wait_free(pe, s_oe, t - 1)
                    b = j % 2
                    for c in range(2):
                        te.matmul(ps_o[b][:, 0:D], aT[b][:, c * P:(c + 1) * P],
                                  w2_sb[:, bass.ds(e * (2 * D) + c * D, D)], start=(c == 0), stop=False)
                    te.matmul(ps_o[b][:, 0:D], ones3[:, :], bias3[:, bass.ds(e * D + NE * 2 * HID, D)],
                              start=False, stop=True).then_inc(s_op, 1)
            run_steps(pe, work, -1, NTILES + 2)


def decay_zero(v, decay, step):
    step(v.memset(decay[:, :], 0.0))
    return decay[:, :]


def ones_like(v, step, over):
    step(v.memset(over[:, 0, 0, :], 1.0))
    return over[:, 0, 0, :]


def positions_table():
    at = np.arange(1, SEQ + 1, dtype=np.float32)[:, None]
    i = np.arange(D)
    exponent = np.where(i % 2 == 0, i, i + 1).astype(np.float32) / np.float32(D)
    angle = (at / np.power(np.float32(10000.0), exponent)).astype(np.float32)
    table = np.where(i % 2 == 0, np.cos(angle), np.sin(angle)).astype(np.float32)
    return np.ascontiguousarray(table.reshape(2, P, D).transpose(1, 0, 2))


def kernel(**inputs):
    import concourse.bacc as bacc
    from concourse.bass_utils import run_bass_kernel_spmd

    x = {k: np.asarray(v) for k, v in inputs.items()}
    lay = np.ascontiguousarray
    arrays = {
        "tok": lay(x["x"].reshape(NT, P).T),
        "emb_table": lay(x["L0_tok_W"].T),
        "emb_b": lay(x["L0_tok_b"]),
        "pos": positions_table(),
        "lam_re": lay(x["L0_attn_Lambda_re"].reshape(-1, 1)),
        "lam_im": lay(x["L0_attn_Lambda_im"].reshape(-1, 1)),
        "log_step": lay(x["L0_attn_log_step"]),
        "b_mat": lay(x["L0_attn_B"].transpose(2, 0, 1)),
        "c_mat": lay(x["L0_attn_C"].transpose(2, 1, 0)),
        "d_vec": lay(x["L0_attn_D"].reshape(-1, 1)),
        "router_w": lay(x["L0_ffn_router_w"].T),
        "router_b": lay(x["L0_ffn_router_b"]),
        "w1": lay(x["L0_ffn_fc1_w"].transpose(2, 0, 1).reshape(D, NE * 2 * HID)),
        "b12": lay(np.concatenate([x["L0_ffn_fc1_b"].reshape(-1, P), x["L0_ffn_fc2_b"].reshape(-1, P)])),
        "w2": lay(x["L0_ffn_fc2_w"].reshape(NE, D, 2, P).transpose(3, 0, 2, 1).reshape(P, NE * 2 * D)),
    }
    nc = bacc.Bacc("TRN2", target_bir_lowering=False, num_devices=1)
    args = [nc.dram_tensor(name, a.shape, mybir.dt.from_np(a.dtype), kind="ExternalInput").ap()
            for name, a in arrays.items()]
    args.append(nc.dram_tensor("out", (8, SEQ, D), F32, kind="ExternalOutput").ap())
    lm_tower(nc, *args)
    return run_bass_kernel_spmd(nc, [arrays], core_ids=[0]).results[0]["out"]
```
